# Optimizing a Trainium2 kernel written in Bass

```python
import numpy as np
import jax
import jax.numpy as jnp

def _softmax(x, axis=-1):
    return jax.nn.softmax(x, axis=axis)

def _gelu(x):
    return jax.nn.gelu(x, approximate=True)

def _silu(x):
    return jax.nn.silu(x)

def _sigmoid(x):
    return jax.nn.sigmoid(x)

def _layernorm(x, axis=-1, eps=1e-05):
    m = jnp.mean(x, axis=axis, keepdims=True)
    v = jnp.var(x, axis=axis, keepdims=True)
    return (x - m) / jnp.sqrt(v + eps)

def _scatter_add(tgt, idx, src, axis=0):
    return tgt.at[idx].add(src)

def _segment_sum(src, seg, n):
    return jax.ops.segment_sum(src, seg, n)
kernel_name = 'mk_adaln_ffn_d1_seqx_r4_7f282e'

def setup_inputs(seed: int=0):
    np.random.seed(seed)
    _w = jnp.asarray

    def _rec_inputs():
        import jax
        import jax.numpy as jnp
        _rk = jax.random.key(seed)
        x = -7.109e-05 + 0.9999 * jax.random.normal(jax.random.fold_in(_rk, 1), (32, 64, 1024), jnp.float32)
        _lenS = 64 - jax.random.randint(jax.random.fold_in(_rk, 7), (32,), 0, max(1, 64 // 4) + 1, jnp.int32)
        _lenS2 = 64 - jax.random.randint(jax.random.fold_in(_rk, 8), (32,), 0, max(1, 64 // 4) + 1, jnp.int32)
        itok_B_0_15 = jax.random.randint(jax.random.fold_in(_rk, 11), (32,), 0, 16, jnp.int32)
        return (x, itok_B_0_15)
    x, itok_B_0_15 = _rec_inputs()

    def _L0_cond_setup():
        import jax, jax.numpy as jnp
        import numpy as np
        B, C, T = (64, 64, 1024)
        S, D = (16, 64)
        key = jax.random.key(seed)
        k1, k2, k3 = jax.random.split(key, 3)
        x = jax.random.normal(k1, (B, C, T), dtype=jnp.float32)
        condition = jax.random.randint(k2, (B,), 0, S, dtype=jnp.int64)
        bound = float(np.sqrt(6.0 / C))
        weights = jax.random.uniform(k3, (S, C, D), dtype=jnp.float32, minval=-bound, maxval=bound)
        return {'x': x, 'condition': condition, 'weights': weights}
    _L0_cond_all = _L0_cond_setup()
    _L0_cond_in = {k: v for k, v in _L0_cond_all.items() if k in ('weights',)}
    del _L0_cond_all

    def _L0_ffn_setup():
        import jax, jax.numpy as jnp
        import numpy as np
        B, S, D, F = (4, 512, 1024, 4096)
        key = jax.random.key(seed)
        k = jax.random.split(key, 5)
        scale_in = 1.0 / np.sqrt(D)
        scale_out = 1.0 / np.sqrt(F)
        return {'input': jax.random.normal(k[0], (B, S, D), dtype=jnp.float32), 'inter_w': jax.random.normal(k[1], (D, F), dtype=jnp.float32) * scale_in, 'inter_b': jax.random.normal(k[2], (F,), dtype=jnp.float32) * 0.02, 'output_w': jax.random.normal(k[3], (F, D), dtype=jnp.float32) * scale_out, 'output_b': jax.random.normal(k[4], (D,), dtype=jnp.float32) * 0.02}
    _L0_ffn_all = _L0_ffn_setup()
    _L0_ffn_in = {k: v for k, v in _L0_ffn_all.items() if k in ('inter_w', 'inter_b', 'output_w', 'output_b')}
    del _L0_ffn_all
    return {'x': x, 'itok_B_0_15': itok_B_0_15, 'L0_cond_weights': _L0_cond_in['weights'], 'L0_ffn_inter_w': _L0_ffn_in['inter_w'], 'L0_ffn_inter_b': _L0_ffn_in['inter_b'], 'L0_ffn_output_w': _L0_ffn_in['output_w'], 'L0_ffn_output_b': _L0_ffn_in['output_b']}

def reference(x, itok_B_0_15, L0_cond_weights, L0_ffn_inter_w, L0_ffn_inter_b, L0_ffn_output_w, L0_ffn_output_b):
    import jax
    import jax.numpy as jnp

    def _L0_cond_ref(x, condition, weights):
        import jax, jax.numpy as jnp
        import numpy as np
        B, C, T = (64, 64, 1024)
        S, D = (16, 64)
        W = weights[condition]
        return jnp.einsum('bct,bcd->bdt', x, W)

    def _L0_ffn_ref(input, inter_w, inter_b, output_w, output_b):
        import jax, jax.numpy as jnp
        import numpy as np
        B, S, D, F = (4, 512, 1024, 4096)
        h = jax.nn.gelu(jnp.einsum('bsd,df->bsf', input, inter_w) + inter_b, approximate=True)
        out = jnp.einsum('bsf,fd->bsd', h, output_w) + output_b
        return out
    x = x + _L0_ffn_ref(_L0_cond_ref(x, itok_B_0_15, L0_cond_weights), L0_ffn_inter_w, L0_ffn_inter_b, L0_ffn_output_w, L0_ffn_output_b)
    return x

_drawn_inputs = setup_inputs


def setup_inputs(seed=0):
    import zlib

    import numpy as np

    out = dict(_drawn_inputs(seed))
    spreads = {}
    factors = {'L0_ffn_inter_b': 5.585, 'L0_ffn_output_b': 3.976}
    for name, (base, spread) in spreads.items():
        noise = np.random.default_rng([zlib.crc32(name.encode()), seed]).standard_normal(out[name].shape)
        drawn = base * np.exp(spread * noise) if base else spread * noise
        out[name] = jnp.asarray(drawn.astype(out[name].dtype))
    for name, factor in factors.items():
        out[name] = (out[name] * factor).astype(out[name].dtype)
    return out
```

```python
from contextlib import ExitStack

import concourse.bass as bass
from concourse import mybir

F32 = mybir.dt.float32
F32R = mybir.dt.float32r
I32 = mybir.dt.int32
ALU = mybir.AluOpType
ACT = mybir.ActivationFunctionType

P = 128
BANK = 512
HALVES = 2
GROUP = 256


def build(nc, x, itok, cond_w, w1, b1, w2, b2, out):
    B, C, D = x.shape
    F = w1.shape[1]
    PER = P // C
    TILES = B // PER // HALVES
    CHUNKS = TILES * P // BANK
    CT = TILES // CHUNKS
    KB = D // P
    DH = D // BANK
    FB = GROUP // P
    NG = F // GROUP
    FT = CHUNKS * FB
    ST = TILES * DH
    CST = ST // CHUNKS
    RING = 4
    YT = CHUNKS * KB
    assert PER == 2 and FT == 4 and CHUNKS == 2 and DH == 2 and FB == 2

    x_tok = x.rearrange("(h j s) c t -> h (s c) j t", h=HALVES, s=PER)
    out_tok = out.rearrange("(h j s) c t -> h (s c) j t", h=HALVES, s=PER)
    w1_v = w1.rearrange("(k p) f -> p k f", p=P)
    w2_v = w2.rearrange("(g b p) d -> g p b d", p=P, b=FB)

    with ExitStack() as ctx:
        def sb(name, shape, dt=F32):
            return ctx.enter_context(nc.sbuf_tensor(name, shape, dt))

        def sem(name):
            return ctx.enter_context(nc.semaphore(name))

        acc = sb("acc", [P, HALVES, TILES, D])
        wdiag = sb("wdiag", [P, TILES, P])
        y_hi = sb("y_hi", [P, KB, TILES * P], F32R)
        y_lo = sb("y_lo", [P, KB, TILES * P], F32R)
        w1_raw = sb("w1_raw", [P, KB, GROUP])
        w1_hi = sb("w1_hi", [P, KB, GROUP], F32R)
        w1_lo = sb("w1_lo", [P, KB, GROUP], F32R)
        w2_raw = sb("w2_raw", [P, FB, D])
        w2_hi = sb("w2_hi", [P, FB, D], F32R)
        w2_lo = sb("w2_lo", [P, FB, D], F32R)
        h_full = sb("h_full", [P, FB, BANK])
        h_hi = sb("h_hi", [P, FB, TILES * P], F32R)
        h_lo = sb("h_lo", [P, FB, TILES * P], F32R)
        b2_all = sb("b2_all", [P, D])
        b1_rows = sb("b1_rows", [F // P, P])
        b1_col = sb("b1_col", [P, F // P])
        b1_now = sb("b1_now", [P, FB])
        ident = sb("ident", [F // P, F // P])
        itok_sb = sb("itok_sb", [1, B], I32)

        first_ps = ctx.enter_context(nc.psum_tensor("first_ps", [P, FT, BANK], F32))
        second_ps = ctx.enter_context(nc.psum_tensor("second_ps", [P, RING, BANK], F32))

        itok_in = sem("itok_in")
        wdiag_in = sem("wdiag_in")
        wdiag_zero = sem("wdiag_zero")
        x_in = [[sem(f"x_in_{h}_{c}") for c in range(CHUNKS)] for h in range(HALVES)]
        b1_in = sem("b1_in")
        b2_in = sem("b2_in")
        w1_in = sem("w1_in")
        w2_in = sem("w2_in")
        ident_zero = sem("ident_zero")
        ident_made = sem("ident_made")
        b1_turned = sem("b1_turned")
        b1_ready = sem("b1_ready")
        b1_set = sem("b1_set")
        cond_done = sem("cond_done")
        y_hi_made = sem("y_hi_made")
        y_ready = sem("y_ready")
        bias_added = sem("bias_added")
        w1_hi_made = sem("w1_hi_made")
        w1_ready = sem("w1_ready")
        w2_hi_made = sem("w2_hi_made")
        w2_ready = sem("w2_ready")
        first_done = sem("first_done")
        gelu_done = sem("gelu_done")
        h_ready = sem("h_ready")
        second_done = sem("second_done")
        acc_added = sem("acc_added")
        out_done = sem("out_done")

        block = ctx.enter_context(nc.Block())

        def chunk(c):
            return slice(c * BANK, (c + 1) * BANK)

        def blk(b):
            return slice(b * P, (b + 1) * P)

        @block.sync
        def _(sp):
            def load_cond(h):
                with sp.Fori(0, TILES) as j:
                    for s in range(PER):
                        which = sp.value_load(itok_sb[0:1, bass.ds(h * TILES * PER + j * PER + s, 1)],
                                              min_val=0, max_val=cond_w.shape[0] - 1)
                        sp.dma_start(wdiag[s * C:(s + 1) * C, bass.ds(j, 1), s * C:(s + 1) * C],
                                     cond_w[bass.ds(which, 1)].rearrange("o c d -> c o d")).then_inc(wdiag_in, 16)

            def load_x(h, c):
                tiles = slice(c * CT, (c + 1) * CT)
                sp.dma_start(acc[:, h, tiles, :], x_tok[h, :, tiles, :]).then_inc(x_in[h][c], 16)

            def load_weights(g, n):
                if not (isinstance(n, int) and n == 0):
                    sp.wait_ge(w1_ready, n * FB)
                sp.dma_start(w1_raw[:], w1_v[:, :, bass.ds(g * GROUP, GROUP)]).then_inc(w1_in, 16)
                if not (isinstance(n, int) and n == 0):
                    sp.wait_ge(w2_ready, n * FB)
                sp.dma_start(w2_raw[:], w2_v[bass.ds(g, 1)].rearrange("o p b d -> p (o b) d")).then_inc(w2_in, 16)

            sp.dma_start(itok_sb[:], itok.rearrange("(o b) -> o b", o=1)).then_inc(itok_in, 16)
            load_x(0, 0)
            sp.wait_ge(itok_in, 16)
            load_cond(0)
            load_weights(0, 0)
            load_x(0, 1)
            load_x(1, 0)
            load_x(1, 1)
            sp.wait_ge(cond_done, YT)
            load_cond(1)
            for h in range(HALVES):
                if h > 0:
                    load_weights(0, h * NG)
                    for j in range(TILES):
                        sp.wait_ge(acc_added, (h * NG - 1) * ST + (j + 1) * DH)
                        sp.dma_start(out_tok[h - 1, :, j, :], acc[:, h - 1, j, :]).then_inc(out_done, 16)
                with sp.Fori(1, NG) as g:
                    load_weights(g, h * NG + g)
            h = HALVES - 1
            for j in range(TILES):
                sp.wait_ge(acc_added, (HALVES * NG - 1) * ST + (j + 1) * DH)
                sp.dma_start(out_tok[h, :, j, :], acc[:, h, j, :]).then_inc(out_done, 16)
            sp.wait_ge(out_done, 16 * HALVES * TILES)

        @block.gpsimd
        def _(pool):
            nc.gpsimd.memset(wdiag[0:C, :, C:P], 0.0).then_inc(wdiag_zero, 1)
            nc.gpsimd.memset(wdiag[C:P, :, 0:C], 0.0).then_inc(wdiag_zero, 1)
            nc.gpsimd.memset(ident[:], 0.0).then_inc(ident_zero, 1)
            pool.wait_ge(ident_zero, 1)
            nc.gpsimd.affine_select(out=ident[:], in_=ident[:], compare_op=ALU.not_equal, fill=1.0, base=0,
                                    pattern=[[-1, F // P]], channel_multiplier=1).then_inc(ident_made, 1)
            pool.wait_ge(b2_in, 16)
            for h in range(HALVES):
                for c in range(CHUNKS):
                    pool.wait_ge(cond_done, h * YT + (c + 1) * KB)
                    for j in range(c * CT, (c + 1) * CT):
                        nc.gpsimd.tensor_tensor(acc[:, h, j, :], acc[:, h, j, :], b2_all[:],
                                                ALU.add).then_inc(bias_added, 1)

        @block.tensor
        def _(pe):
            def cond(h, c):
                pe.wait_ge(x_in[h][c], 16)
                if c == 0:
                    pe.wait_ge(wdiag_in, (h + 1) * 16 * TILES * PER)
                    if h > 0:
                        pe.wait_ge(gelu_done, h * NG * FT)
                else:
                    if h > 0:
                        pe.wait_ge(acc_added, h * NG * ST)
                banks = first_ps if c == 0 else second_ps
                for k in range(KB):
                    if k >= RING:
                        pe.wait_ge(y_ready, h * YT + c * KB + k - RING + 1)
                    for j in range(CT):
                        last = nc.tensor.matmul(banks[:, k % RING, blk(j)], acc[:, h, c * CT + j, blk(k)],
                                                wdiag[:, c * CT + j, :], start=True, stop=True)
                    last.then_inc(cond_done, 1)

            def first(n, c, b):
                for k in range(KB):
                    for i, (w, y) in enumerate(((w1_hi, y_hi), (w1_hi, y_lo), (w1_lo, y_hi))):
                        last = nc.tensor.matmul(first_ps[:, c * FB + b, :], w[:, k, blk(b)], y[:, k, chunk(c)],
                                                start=(k == 0 and i == 0), stop=(k == KB - 1 and i == 2))
                last.then_inc(first_done, 1)

            def first_of_half(h):
                n = h * NG
                for c in range(CHUNKS):
                    if c > 0:
                        cond(h, c)
                    for b in range(FB):
                        pe.wait_ge(y_ready, h * YT + (c + 1) * KB)
                        if c == 0:
                            pe.wait_ge(w1_ready, n * FB + b + 1)
                        elif n > 0:
                            pe.wait_ge(gelu_done, (n - 1) * FT + c * FB + b + 1)
                        first(n, c, b)

            def first_of_group(n):
                for c in range(CHUNKS):
                    for b in range(FB):
                        if c == 0:
                            pe.wait_ge(w1_ready, n * FB + b + 1)
                        pe.wait_ge(gelu_done, (n - 1) * FT + c * FB + b + 1)
                        first(n, c, b)

            def second(n):
                pe.wait_ge(w2_ready, (n + 1) * FB)
                for t in range(ST):
                    j, d = divmod(t, DH)
                    if t % CST == 0:
                        pe.wait_ge(h_ready, n * FT + (t // CST + 1) * FB)
                    if not (isinstance(n, int) and n == 0 and t < RING):
                        pe.wait_ge(acc_added, n * ST + t - RING + 1)
                    for b in range(FB):
                        for i, (a, w) in enumerate(((h_hi, w2_hi), (h_hi, w2_lo), (h_lo, w2_hi))):
                            last = nc.tensor.matmul(second_ps[:, t % RING, :], a[:, b, blk(j)], w[:, b, chunk(d)],
                                                    start=(b == 0 and i == 0), stop=(b == FB - 1 and i == 2))
                    last.then_inc(second_done, 1)

            pe.wait_ge(b1_in, 16)
            pe.wait_ge(ident_made, 1)
            nc.tensor.matmul(second_ps[:, 0, 0:F // P], b1_rows[:], ident[:], start=True, stop=True).then_inc(b1_turned, 1)
            pe.wait_ge(wdiag_zero, 2)
            cond(0, 0)
            pe.wait_ge(b1_ready, 1)
            for h in range(HALVES):
                first_of_half(h)
                first_n = h * NG
                if h == 0:
                    second(0)
                    first_of_group(1)
                    first_n = 1
                with pe.Fori(first_n, h * NG + NG - 1) as n:
                    second(n)
                    first_of_group(n + 1)
                if h + 1 < HALVES:
                    cond(h + 1, 0)
                second(h * NG + NG - 1)

        @block.scalar
        def _(act):
            def y_parts(h, c):
                if h > 0:
                    act.wait_ge(first_done, h * NG * FT)
                banks = first_ps if c == 0 else second_ps
                for k in range(KB):
                    act.wait_ge(cond_done, h * YT + c * KB + k + 1)
                    nc.scalar.activation(y_hi[:, k, chunk(c)], banks[:, k % RING, :], ACT.Copy).then_inc(y_hi_made, 1)

            def w1_parts(n):
                act.wait_ge(w1_in, (n + 1) * 16)
                for b in range(FB):
                    if not (isinstance(n, int) and n == 0):
                        act.wait_ge(first_done, n * FT - FB + b + 1)
                    nc.scalar.activation(w1_hi[:, :, blk(b)], w1_raw[:, :, blk(b)], ACT.Copy).then_inc(w1_hi_made, 1)

            def w2_parts(n):
                act.wait_ge(w2_in, (n + 1) * 16)
                if not (isinstance(n, int) and n == 0):
                    act.wait_ge(second_done, n * ST)
                for b in range(FB):
                    nc.scalar.activation(w2_hi[:, b, :], w2_raw[:, b, :], ACT.Copy).then_inc(w2_hi_made, 1)

            def gelu(n, c):
                act.wait_ge(b1_set, n + 1)
                for b in range(FB):
                    act.wait_ge(first_done, n * FT + c * FB + b + 1)
                    if not (isinstance(n, int) and n == 0):
                        act.wait_ge(second_done, (n - 1) * ST + (c + 1) * CST)
                    if not (isinstance(n, int) and n == 0 and c == 0):
                        act.wait_ge(h_ready, n * FT + c * FB + b - FB + 1)
                    bias = b1_now[:, b:b + 1]
                    nc.scalar.activation(h_hi[:, b, chunk(c)], first_ps[:, c * FB + b, :], ACT.Gelu_apprx_tanh, bias=bias)
                    nc.scalar.activation(h_full[:, b, :], first_ps[:, c * FB + b, :], ACT.Gelu_apprx_tanh,
                                         bias=bias).then_inc(gelu_done, 1)

            act.dma_start(b1_rows[:], b1.rearrange("(a p) -> a p", p=P)).then_inc(b1_in, 16)
            act.dma_start(b2_all[:], b2.partition_broadcast(P)).then_inc(b2_in, 16)
            for h in range(HALVES):
                n = h * NG
                y_parts(h, 0)
                w1_parts(n)
                gelu(n, 0)
                y_parts(h, 1)
                w2_parts(n)
                gelu(n, 1)
                with act.Fori(1, NG) as g:
                    w1_parts(h * NG + g)
                    w2_parts(h * NG + g)
                    for c in range(CHUNKS):
                        gelu(h * NG + g, c)

        @block.vector
        def _(dve):
            def y_parts(h, c):
                banks = first_ps if c == 0 else second_ps
                for k in range(KB):
                    dve.wait_ge(y_hi_made, h * YT + c * KB + k + 1)
                    nc.vector.tensor_tensor(y_lo[:, k, chunk(c)], banks[:, k % RING, :], y_hi[:, k, chunk(c)].bitcast(F32),
                                            ALU.subtract).then_inc(y_ready, 1)

            def w1_part(n, b):
                dve.wait_ge(w1_hi_made, n * FB + b + 1)
                nc.vector.tensor_tensor(w1_lo[:, :, blk(b)], w1_raw[:, :, blk(b)], w1_hi[:, :, blk(b)].bitcast(F32),
                                        ALU.subtract).then_inc(w1_ready, 1)

            def w2_part(n, b):
                dve.wait_ge(w2_hi_made, n * FB + b + 1)
                nc.vector.tensor_tensor(w2_lo[:, b, :], w2_raw[:, b, :], w2_hi[:, b, :].bitcast(F32),
                                        ALU.subtract).then_inc(w2_ready, 1)

            def h_part(n, c, b):
                dve.wait_ge(gelu_done, n * FT + c * FB + b + 1)
                nc.vector.tensor_tensor(h_lo[:, b, chunk(c)], h_full[:, b, :], h_hi[:, b, chunk(c)].bitcast(F32),
                                        ALU.subtract).then_inc(h_ready, 1)

            def add(n, h, t):
                j, d = divmod(t, DH)
                dve.wait_ge(second_done, n * ST + t + 1)
                nc.vector.tensor_tensor(acc[:, h, j, chunk(d)], second_ps[:, t % RING, :], acc[:, h, j, chunk(d)],
                                        ALU.add).then_inc(acc_added, 1)

            def add_and_split(n, h):
                for t in range(ST):
                    add(n, h, t)
                    if t % RING == RING - 1 and t // RING < FB:
                        w1_part(n + 1, t // RING)

            def set_b1(g):
                nc.vector.tensor_copy(b1_now[:], b1_col[:, bass.ds(g * FB, FB)]).then_inc(b1_set, 1)

            dve.wait_ge(b1_turned, 1)
            nc.vector.tensor_copy(b1_col[:], second_ps[:, 0, 0:F // P]).then_inc(b1_ready, 1)
            for h in range(HALVES):
                n = h * NG
                if h == 0:
                    dve.wait_ge(b1_ready, 1)
                set_b1(0)
                y_parts(h, 0)
                if h == 0:
                    w1_part(0, 0)
                    w1_part(0, 1)
                else:
                    add_and_split(n - 1, h - 1)
                h_part(n, 0, 0)
                h_part(n, 0, 1)
                y_parts(h, 1)
                w2_part(n, 0)
                w2_part(n, 1)
                h_part(n, 1, 0)
                h_part(n, 1, 1)
                dve.wait_ge(bias_added, (h + 1) * TILES)
                with dve.Fori(1, NG) as g:
                    n = h * NG + g
                    set_b1(g)
                    add_and_split(n - 1, h)
                    w2_part(n, 0)
                    h_part(n, 0, 0)
                    w2_part(n, 1)
                    h_part(n, 0, 1)
                    h_part(n, 1, 0)
                    h_part(n, 1, 1)
            for t in range(ST):
                add(HALVES * NG - 1, HALVES - 1, t)


_INS = ["x", "itok_B_0_15", "L0_cond_weights", "L0_ffn_inter_w", "L0_ffn_inter_b", "L0_ffn_output_w", "L0_ffn_output_b"]


def kernel(**inputs):
    import numpy as _np
    import concourse.bacc as _bacc
    from concourse import mybir as _mybir
    from concourse.bass_utils import run_bass_kernel_spmd as _run

    nc = _bacc.Bacc("TRN2", target_bir_lowering=False, num_devices=1)
    arrays, args = {}, []
    for name in _INS:
        a = _np.ascontiguousarray(inputs[name])
        arrays[f"in_{name}_dram"] = a
        args.append(nc.dram_tensor(f"in_{name}_dram", a.shape, _mybir.dt.from_np(a.dtype), kind="ExternalInput").ap())
    out = nc.dram_tensor("out_dram", arrays["in_x_dram"].shape, F32, kind="ExternalOutput").ap()
    build(nc, *args, out)
    r = _run(nc, [arrays], core_ids=[0])
    return r.results[0]["out_dram"]
```

```python
from contextlib import ExitStack

import concourse.bass as bass
from concourse import mybir

F32 = mybir.dt.float32
F32R = mybir.dt.float32r
I32 = mybir.dt.int32
ALU = mybir.AluOpType
ACT = mybir.ActivationFunctionType

P = 128
BANK = 512
HALVES = 2
GROUP = 256


def build(nc, x, itok, cond_w, w1, b1, w2, b2, out):
    B, C, D = x.shape
    SETS = cond_w.shape[0]
    F = w1.shape[1]
    PER = P // C
    TILES = B // PER // HALVES
    CHUNKS = TILES * P // BANK
    CT = TILES // CHUNKS
    KB = D // P
    DH = D // BANK
    FB = GROUP // P
    NG = F // GROUP
    FT = CHUNKS * FB
    ST = TILES * DH
    CST = ST // CHUNKS
    RING = 4
    YB = BANK // P
    YC = CT * KB // YB
    YT = CHUNKS * YC
    assert PER == 2 and FT == 4 and CHUNKS == 2 and DH == 2 and FB == 2

    x_tok = x.rearrange("(h j s) c t -> h (s c) j t", h=HALVES, s=PER)
    out_tok = out.rearrange("(h j s) c t -> h (s c) j t", h=HALVES, s=PER)
    w1_v = w1.rearrange("(k p) f -> p k f", p=P)
    w2_v = w2.rearrange("(g b p) d -> g p b d", p=P, b=FB)

    with ExitStack() as ctx:
        def sb(name, shape, dt=F32):
            return ctx.enter_context(nc.sbuf_tensor(name, shape, dt))

        def sem(name):
            return ctx.enter_context(nc.semaphore(name))

        acc = sb("acc", [P, HALVES, TILES, D])
        cond_all = sb("cond_all", [P, SETS, C])
        wdiag = sb("wdiag", [P, TILES, P])
        y_hi = sb("y_hi", [P, KB, TILES * P], F32R)
        y_lo = sb("y_lo", [P, KB, TILES * P], F32R)
        w1_raw = sb("w1_raw", [P, KB, GROUP])
        w1_hi = sb("w1_hi", [P, KB, GROUP], F32R)
        w1_lo = sb("w1_lo", [P, KB, GROUP], F32R)
        w2_raw = sb("w2_raw", [P, FB, D])
        w2_hi = sb("w2_hi", [P, FB, D], F32R)
        w2_lo = sb("w2_lo", [P, FB, D], F32R)
        h_full = sb("h_full", [P, BANK])
        h_hi = sb("h_hi", [P, FB, TILES * P], F32R)
        h_lo = sb("h_lo", [P, FB, TILES * P], F32R)
        b2_all = sb("b2_all", [P, D])
        b1_rows = sb("b1_rows", [F // P, P])
        b1_col = sb("b1_col", [P, F // P])
        b1_now = sb("b1_now", [P, FB])
        ident = sb("ident", [F // P, F // P])
        itok_sb = sb("itok_sb", [1, B], I32)

        first_ps = ctx.enter_context(nc.psum_tensor("first_ps", [P, FT, BANK], F32))
        second_ps = ctx.enter_context(nc.psum_tensor("second_ps", [P, RING, BANK], F32))

        itok_in = sem("itok_in")
        cond_in = sem("cond_in")
        wdiag_set = sem("wdiag_set")
        wdiag_zero = sem("wdiag_zero")
        x_in = [[sem(f"x_in_{h}_{j}") for j in range(TILES)] for h in range(HALVES)]
        b1_in = sem("b1_in")
        b2_in = sem("b2_in")
        w1_start_in = [sem(f"w1_start_in_{b}") for b in range(FB)]
        w1_in = sem("w1_in")
        w2_in = sem("w2_in")
        ident_zero = sem("ident_zero")
        ident_made = sem("ident_made")
        b1_turned = sem("b1_turned")
        b1_ready = sem("b1_ready")
        b1_set = sem("b1_set")
        cond_done = sem("cond_done")
        y_hi_made = sem("y_hi_made")
        y_ready = sem("y_ready")
        bias_added = sem("bias_added")
        w1_hi_made = sem("w1_hi_made")
        w1_ready = sem("w1_ready")
        w2_hi_made = sem("w2_hi_made")
        w2_ready = sem("w2_ready")
        first_done = sem("first_done")
        gelu_done = sem("gelu_done")
        h_ready = sem("h_ready")
        second_done = sem("second_done")
        acc_added = sem("acc_added")
        out_done = sem("out_done")

        block = ctx.enter_context(nc.Block())

        def chunk(c):
            return slice(c * BANK, (c + 1) * BANK)

        def blk(b):
            return slice(b * P, (b + 1) * P)

        def y_bank(u):
            return (first_ps if u < YC else second_ps)[:, u % RING, :].rearrange("p (k t) -> p k t", k=YB)

        def y_of(part, u):
            j, q = divmod(u, KB // YB)
            return part[:, q * YB:(q + 1) * YB, blk(j)]

        @block.sync
        def _(sp):
            def load_x(h, j):
                sp.dma_start(acc[:, h, j, :], x_tok[h, :, j, :]).then_inc(x_in[h][j], 16)

            def load_w1(g, n):
                sp.wait_ge(w1_ready, n * FB)
                sp.dma_start(w1_raw[:], w1_v[:, :, bass.ds(g * GROUP, GROUP)]).then_inc(w1_in, 16)

            def load_w2(g, n):
                if not (isinstance(n, int) and n == 0):
                    sp.wait_ge(w2_ready, n * FB)
                sp.dma_start(w2_raw[:], w2_v[bass.ds(g, 1)].rearrange("o p b d -> p (o b) d")).then_inc(w2_in, 16)

            sp.dma_start(itok_sb[:], itok.rearrange("(o b) -> o b", o=1)).then_inc(itok_in, 16)
            sp.dma_start(cond_all[0:C], cond_w.rearrange("s c d -> c s d")).then_inc(cond_in, 16)
            for b in range(FB):
                for j in range(b * CT // FB, (b + 1) * CT // FB):
                    load_x(0, j)
                sp.dma_start(w1_raw[:, :, blk(b)], w1_v[:, :, blk(b)]).then_inc(w1_start_in[b], 16)
            for j in range(CT, TILES):
                load_x(0, j)
            load_w2(0, 0)
            sp.dma_start(b2_all[:], b2.partition_broadcast(P)).then_inc(b2_in, 16)
            load_w1(1, 1)
            for j in range(TILES):
                load_x(1, j)
            load_w2(1, 1)
            for h in range(HALVES):
                if h > 0:
                    load_w1(0, h * NG)
                    load_w2(0, h * NG)
                    for j in range(TILES):
                        sp.wait_ge(acc_added, (h * NG - 1) * ST + (j + 1) * DH)
                        sp.dma_start(out_tok[h - 1, :, j, :], acc[:, h - 1, j, :]).then_inc(out_done, 16)
                with sp.Fori(2 if h == 0 else 1, NG) as g:
                    load_w1(g, h * NG + g)
                    load_w2(g, h * NG + g)
            h = HALVES - 1
            for j in range(TILES):
                sp.wait_ge(acc_added, (HALVES * NG - 1) * ST + (j + 1) * DH)
                sp.dma_start(out_tok[h, :, j, :], acc[:, h, j, :]).then_inc(out_done, 16)
            sp.wait_ge(out_done, 16 * HALVES * TILES)

        @block.gpsimd
        def _(pool):
            nc.gpsimd.memset(wdiag[0:C, :, C:P], 0.0).then_inc(wdiag_zero, 1)
            nc.gpsimd.memset(wdiag[C:P, :, 0:C], 0.0).then_inc(wdiag_zero, 1)
            nc.gpsimd.memset(ident[:], 0.0).then_inc(ident_zero, 1)
            pool.wait_ge(ident_zero, 1)
            nc.gpsimd.affine_select(out=ident[:], in_=ident[:], compare_op=ALU.not_equal, fill=1.0, base=0,
                                    pattern=[[-1, F // P]], channel_multiplier=1).then_inc(ident_made, 1)

            def pick_cond(h):
                with pool.Fori(0, TILES) as j:
                    for s in range(PER):
                        which = pool.value_load(itok_sb[0:1, bass.ds((h * TILES + j) * PER + s, 1)],
                                                min_val=0, max_val=SETS - 1)
                        rows = slice(s * C, (s + 1) * C)
                        nc.gpsimd.tensor_copy(wdiag[rows, bass.ds(j, 1), rows],
                                              cond_all[rows, bass.ds(which, 1), :]).then_inc(wdiag_set, 1)
                pool.wait_ge(wdiag_set, (h + 1) * TILES * PER)

            pool.wait_ge(itok_in, 16)
            pool.wait_ge(cond_in, 32)
            pick_cond(0)
            pool.wait_ge(b2_in, 16)
            for h in range(HALVES):
                for c in range(CHUNKS):
                    pool.wait_ge(cond_done, h * YT + (c + 1) * YC)
                    for j in range(c * CT, (c + 1) * CT):
                        nc.gpsimd.tensor_tensor(acc[:, h, j, :], acc[:, h, j, :], b2_all[:],
                                                ALU.add).then_inc(bias_added, 1)
                if h + 1 < HALVES:
                    pool.wait_ge(bias_added, (h + 1) * TILES)
                    pick_cond(h + 1)

        @block.tensor
        def _(pe):
            def cond(h, c):
                if h > 0:
                    if c == 0:
                        pe.wait_ge(gelu_done, h * NG * FT)
                    else:
                        pe.wait_ge(acc_added, h * NG * ST)
                banks = first_ps if c == 0 else second_ps
                for j in range(c * CT, (c + 1) * CT):
                    pe.wait_ge(x_in[h][j], 16)
                    pe.wait_ge(wdiag_set, (h * TILES + j + 1) * PER)
                    for q in range(KB // YB):
                        u = j * KB // YB + q
                        if u % YC >= RING:
                            pe.wait_ge(y_ready, h * YT + u - RING + 1)
                        for k in range(YB):
                            last = nc.tensor.matmul(banks[:, u % RING, blk(k)], acc[:, h, j, blk(q * YB + k)],
                                                    wdiag[:, j, :], start=True, stop=True)
                        last.then_inc(cond_done, 1)

            def first(n, c, b):
                for k in range(KB):
                    for i, (w, y) in enumerate(((w1_hi, y_hi), (w1_hi, y_lo), (w1_lo, y_hi))):
                        last = nc.tensor.matmul(first_ps[:, c * FB + b, :], w[:, k, blk(b)], y[:, k, chunk(c)],
                                                start=(k == 0 and i == 0), stop=(k == KB - 1 and i == 2))
                last.then_inc(first_done, 1)

            def first_of_half(h):
                n = h * NG
                for c in range(CHUNKS):
                    for b in range(FB):
                        pe.wait_ge(y_ready, h * YT + (c + 1) * YC)
                        if c == 0:
                            pe.wait_ge(w1_ready, n * FB + b + 1)
                        elif n > 0:
                            pe.wait_ge(gelu_done, (n - 1) * FT + c * FB + b + 1)
                        first(n, c, b)
                        if c == 0 and b == 0:
                            cond(h, 1)

            def first_of_group(n):
                for c in range(CHUNKS):
                    for b in range(FB):
                        if c == 0:
                            pe.wait_ge(w1_ready, n * FB + b + 1)
                        pe.wait_ge(gelu_done, (n - 1) * FT + c * FB + b + 1)
                        first(n, c, b)

            def second(n):
                pe.wait_ge(w2_ready, (n + 1) * FB)
                for t in range(ST):
                    j, d = divmod(t, DH)
                    if t % CST == 0:
                        pe.wait_ge(h_ready, n * FT + (t // CST + 1) * FB)
                    if not (isinstance(n, int) and n == 0 and t < RING):
                        pe.wait_ge(acc_added, n * ST + t - RING + 1)
                    for b in range(FB):
                        for i, (a, w) in enumerate(((h_hi, w2_hi), (h_hi, w2_lo), (h_lo, w2_hi))):
                            last = nc.tensor.matmul(second_ps[:, t % RING, :], a[:, b, blk(j)], w[:, b, chunk(d)],
                                                    start=(b == 0 and i == 0), stop=(b == FB - 1 and i == 2))
                    last.then_inc(second_done, 1)

            pe.wait_ge(b1_in, 16)
            pe.wait_ge(ident_made, 1)
            nc.tensor.matmul(second_ps[:, 0, 0:F // P], b1_rows[:], ident[:], start=True, stop=True).then_inc(b1_turned, 1)
            pe.wait_ge(wdiag_zero, 2)
            cond(0, 0)
            pe.wait_ge(b1_ready, 1)
            for h in range(HALVES):
                first_of_half(h)
                first_n = h * NG
                if h == 0:
                    second(0)
                    first_of_group(1)
                    first_n = 1
                with pe.Fori(first_n, h * NG + NG - 1) as n:
                    second(n)
                    first_of_group(n + 1)
                if h + 1 < HALVES:
                    cond(h + 1, 0)
                second(h * NG + NG - 1)

        @block.scalar
        def _(act):
            def y_parts(h, units):
                if h > 0:
                    act.wait_ge(first_done, h * NG * FT)
                for u in units:
                    act.wait_ge(cond_done, h * YT + u + 1)
                    nc.scalar.activation(y_of(y_hi, u), y_bank(u), ACT.Copy).then_inc(y_hi_made, 1)

            def w1_part(n, b):
                if isinstance(n, int) and n == 0:
                    act.wait_ge(w1_start_in[b], 16)
                else:
                    if b == 0:
                        act.wait_ge(w1_in, n * 16)
                    act.wait_ge(first_done, n * FT - FB + b + 1)
                nc.scalar.activation(w1_hi[:, :, blk(b)], w1_raw[:, :, blk(b)], ACT.Copy).then_inc(w1_hi_made, 1)

            def w2_parts(n):
                act.wait_ge(w2_in, (n + 1) * 16)
                if not (isinstance(n, int) and n == 0):
                    act.wait_ge(second_done, n * ST)
                for b in range(FB):
                    nc.scalar.activation(w2_hi[:, b, :], w2_raw[:, b, :], ACT.Copy).then_inc(w2_hi_made, 1)

            def gelu(n, c, b):
                act.wait_ge(b1_set, n + 1)
                act.wait_ge(first_done, n * FT + c * FB + b + 1)
                if not (isinstance(n, int) and n == 0):
                    act.wait_ge(second_done, (n - 1) * ST + (c + 1) * CST)
                if not (isinstance(n, int) and n == 0 and c == 0 and b == 0):
                    act.wait_ge(h_ready, n * FT + c * FB + b)
                tile = first_ps[:, c * FB + b, :]
                bias = b1_now[:, b:b + 1]
                nc.scalar.activation(h_hi[:, b, chunk(c)], tile, ACT.Gelu_apprx_tanh, bias=bias)
                nc.scalar.activation(h_full[:], tile, ACT.Gelu_apprx_tanh, bias=bias).then_inc(gelu_done, 1)

            act.dma_start(cond_all[C:P], cond_w.rearrange("s c d -> c s d")).then_inc(cond_in, 16)
            act.dma_start(b1_rows[:], b1.rearrange("(a p) -> a p", p=P)).then_inc(b1_in, 16)
            for h in range(HALVES):
                n = h * NG
                for b in range(FB):
                    y_parts(h, range(b * YC // FB, (b + 1) * YC // FB))
                    w1_part(n, b)
                gelu(n, 0, 0)
                y_parts(h, range(YC, YT))
                gelu(n, 0, 1)
                w2_parts(n)
                gelu(n, 1, 0)
                gelu(n, 1, 1)
                with act.Fori(1, NG) as g:
                    n = h * NG + g
                    for b in range(FB):
                        w1_part(n, b)
                    w2_parts(n)
                    for c in range(CHUNKS):
                        for b in range(FB):
                            gelu(n, c, b)

        @block.vector
        def _(dve):
            def y_parts(h, units):
                for u in units:
                    dve.wait_ge(y_hi_made, h * YT + u + 1)
                    nc.vector.tensor_tensor(y_of(y_lo, u), y_bank(u), y_of(y_hi, u).bitcast(F32),
                                            ALU.subtract).then_inc(y_ready, 1)

            def w1_part(n, b):
                dve.wait_ge(w1_hi_made, n * FB + b + 1)
                nc.vector.tensor_tensor(w1_lo[:, :, blk(b)], w1_raw[:, :, blk(b)], w1_hi[:, :, blk(b)].bitcast(F32),
                                        ALU.subtract).then_inc(w1_ready, 1)

            def w2_part(n, b):
                dve.wait_ge(w2_hi_made, n * FB + b + 1)
                nc.vector.tensor_tensor(w2_lo[:, b, :], w2_raw[:, b, :], w2_hi[:, b, :].bitcast(F32),
                                        ALU.subtract).then_inc(w2_ready, 1)

            def h_part(n, c, b):
                dve.wait_ge(gelu_done, n * FT + c * FB + b + 1)
                nc.vector.tensor_tensor(h_lo[:, b, chunk(c)], h_full[:], h_hi[:, b, chunk(c)].bitcast(F32),
                                        ALU.subtract).then_inc(h_ready, 1)

            def add(n, h, t):
                j, d = divmod(t, DH)
                dve.wait_ge(second_done, n * ST + t + 1)
                nc.vector.tensor_tensor(acc[:, h, j, chunk(d)], second_ps[:, t % RING, :], acc[:, h, j, chunk(d)],
                                        ALU.add).then_inc(acc_added, 1)

            def add_and_split(n, h):
                for t in range(ST):
                    add(n, h, t)
                    if t % RING == RING - 1 and t // RING < FB:
                        w1_part(n + 1, t // RING)

            def set_b1(g):
                nc.vector.tensor_copy(b1_now[:], b1_col[:, bass.ds(g * FB, FB)]).then_inc(b1_set, 1)

            dve.wait_ge(b1_turned, 1)
            nc.vector.tensor_copy(b1_col[:], second_ps[:, 0, 0:F // P]).then_inc(b1_ready, 1)
            for h in range(HALVES):
                n = h * NG
                if h == 0:
                    dve.wait_ge(b1_ready, 1)
                set_b1(0)
                for b in range(FB):
                    y_parts(h, range(b * YC // FB, (b + 1) * YC // FB))
                    if h == 0:
                        w1_part(0, b)
                if h > 0:
                    add_and_split(n - 1, h - 1)
                h_part(n, 0, 0)
                y_parts(h, range(YC, YT))
                h_part(n, 0, 1)
                w2_part(n, 0)
                w2_part(n, 1)
                h_part(n, 1, 0)
                h_part(n, 1, 1)
                dve.wait_ge(bias_added, (h + 1) * TILES)
                with dve.Fori(1, NG) as g:
                    n = h * NG + g
                    set_b1(g)
                    add_and_split(n - 1, h)
                    w2_part(n, 0)
                    h_part(n, 0, 0)
                    w2_part(n, 1)
                    h_part(n, 0, 1)
                    h_part(n, 1, 0)
                    h_part(n, 1, 1)
            for t in range(ST):
                add(HALVES * NG - 1, HALVES - 1, t)


_INS = ["x", "itok_B_0_15", "L0_cond_weights", "L0_ffn_inter_w", "L0_ffn_inter_b", "L0_ffn_output_w", "L0_ffn_output_b"]


def kernel(**inputs):
    import numpy as _np
    import concourse.bacc as _bacc
    from concourse import mybir as _mybir
    from concourse.bass_utils import run_bass_kernel_spmd as _run

    nc = _bacc.Bacc("TRN2", target_bir_lowering=False, num_devices=1)
    arrays, args = {}, []
    for name in _INS:
        a = _np.ascontiguousarray(inputs[name])
        arrays[f"in_{name}_dram"] = a
        args.append(nc.dram_tensor(f"in_{name}_dram", a.shape, _mybir.dt.from_np(a.dtype), kind="ExternalInput").ap())
    out = nc.dram_tensor("out_dram", arrays["in_x_dram"].shape, F32, kind="ExternalOutput").ap()
    build(nc, *args, out)
    r = _run(nc, [arrays], core_ids=[0])
    return r.results[0]["out_dram"]
```
